# Optimizing a Trainium2 kernel written in Bass

```python
import numpy as np
import jax
import jax.numpy as jnp

def _softmax(x, axis=-1):
    return jax.nn.softmax(x, axis=axis)

def _gelu(x):
    return jax.nn.gelu(x, approximate=True)

def _silu(x):
    return jax.nn.silu(x)

def _sigmoid(x):
    return jax.nn.sigmoid(x)

def _layernorm(x, axis=-1, eps=1e-05):
    m = jnp.mean(x, axis=axis, keepdims=True)
    v = jnp.var(x, axis=axis, keepdims=True)
    return (x - m) / jnp.sqrt(v + eps)

def _scatter_add(tgt, idx, src, axis=0):
    return tgt.at[idx].add(src)

def _segment_sum(src, seg, n):
    return jax.ops.segment_sum(src, seg, n)
kernel_name = 'mk_dlrm_tower_d1_rec_r8_edc466'

def setup_inputs(seed: int=0):
    np.random.seed(seed)
    _w = jnp.asarray

    def _rec_inputs():
        import jax
        import jax.numpy as jnp
        _tk = jax.random.key(seed)
        dense_ctx = jax.random.normal(jax.random.fold_in(_tk, 190), (2048, 16), jnp.float32)
        ids = jnp.stack([jax.random.randint(jax.random.fold_in(_tk, 200 + f), (2048,), 0, v, jnp.int32) for f, v in enumerate([12500, 1000, 12500, 1250, 1250, 12500, 12500, 12500, 1250, 1000, 12500, 12500, 1000, 1250, 125000, 12500, 12500, 1250, 12500, 1250, 1000, 125000, 1000, 12500, 1250, 1000, 12500, 1000, 1250, 12500, 12500, 12500])], axis=1)
        tbl_0 = 0.05 * jax.random.normal(jax.random.fold_in(_tk, 500 + 0), (12500, 64), jnp.float32)
        tbl_1 = 0.05 * jax.random.normal(jax.random.fold_in(_tk, 500 + 1), (1000, 64), jnp.float32)
        tbl_2 = 0.05 * jax.random.normal(jax.random.fold_in(_tk, 500 + 2), (12500, 64), jnp.float32)
        tbl_3 = 0.05 * jax.random.normal(jax.random.fold_in(_tk, 500 + 3), (1250, 64), jnp.float32)
        tbl_4 = 0.05 * jax.random.normal(jax.random.fold_in(_tk, 500 + 4), (1250, 64), jnp.float32)
        tbl_5 = 0.05 * jax.random.normal(jax.random.fold_in(_tk, 500 + 5), (12500, 64), jnp.float32)
        tbl_6 = 0.05 * jax.random.normal(jax.random.fold_in(_tk, 500 + 6), (12500, 64), jnp.float32)
        tbl_7 = 0.05 * jax.random.normal(jax.random.fold_in(_tk, 500 + 7), (12500, 64), jnp.float32)
        tbl_8 = 0.05 * jax.random.normal(jax.random.fold_in(_tk, 500 + 8), (1250, 64), jnp.float32)
        tbl_9 = 0.05 * jax.random.normal(jax.random.fold_in(_tk, 500 + 9), (1000, 64), jnp.float32)
        tbl_10 = 0.05 * jax.random.normal(jax.random.fold_in(_tk, 500 + 10), (12500, 64), jnp.float32)
        tbl_11 = 0.05 * jax.random.normal(jax.random.fold_in(_tk, 500 + 11), (12500, 64), jnp.float32)
        tbl_12 = 0.05 * jax.random.normal(jax.random.fold_in(_tk, 500 + 12), (1000, 64), jnp.float32)
        tbl_13 = 0.05 * jax.random.normal(jax.random.fold_in(_tk, 500 + 13), (1250, 64), jnp.float32)
        tbl_14 = 0.05 * jax.random.normal(jax.random.fold_in(_tk, 500 + 14), (125000, 64), jnp.float32)
        tbl_15 = 0.05 * jax.random.normal(jax.random.fold_in(_tk, 500 + 15), (12500, 64), jnp.float32)
        tbl_16 = 0.05 * jax.random.normal(jax.random.fold_in(_tk, 500 + 16), (12500, 64), jnp.float32)
        tbl_17 = 0.05 * jax.random.normal(jax.random.fold_in(_tk, 500 + 17), (1250, 64), jnp.float32)
        tbl_18 = 0.05 * jax.random.normal(jax.random.fold_in(_tk, 500 + 18), (12500, 64), jnp.float32)
        tbl_19 = 0.05 * jax.random.normal(jax.random.fold_in(_tk, 500 + 19), (1250, 64), jnp.float32)
        tbl_20 = 0.05 * jax.random.normal(jax.random.fold_in(_tk, 500 + 20), (1000, 64), jnp.float32)
        tbl_21 = 0.05 * jax.random.normal(jax.random.fold_in(_tk, 500 + 21), (125000, 64), jnp.float32)
        tbl_22 = 0.05 * jax.random.normal(jax.random.fold_in(_tk, 500 + 22), (1000, 64), jnp.float32)
        tbl_23 = 0.05 * jax.random.normal(jax.random.fold_in(_tk, 500 + 23), (12500, 64), jnp.float32)
        tbl_24 = 0.05 * jax.random.normal(jax.random.fold_in(_tk, 500 + 24), (1250, 64), jnp.float32)
        tbl_25 = 0.05 * jax.random.normal(jax.random.fold_in(_tk, 500 + 25), (1000, 64), jnp.float32)
        tbl_26 = 0.05 * jax.random.normal(jax.random.fold_in(_tk, 500 + 26), (12500, 64), jnp.float32)
        tbl_27 = 0.05 * jax.random.normal(jax.random.fold_in(_tk, 500 + 27), (1000, 64), jnp.float32)
        tbl_28 = 0.05 * jax.random.normal(jax.random.fold_in(_tk, 500 + 28), (1250, 64), jnp.float32)
        tbl_29 = 0.05 * jax.random.normal(jax.random.fold_in(_tk, 500 + 29), (12500, 64), jnp.float32)
        tbl_30 = 0.05 * jax.random.normal(jax.random.fold_in(_tk, 500 + 30), (12500, 64), jnp.float32)
        tbl_31 = 0.05 * jax.random.normal(jax.random.fold_in(_tk, 500 + 31), (12500, 64), jnp.float32)
        _rk = jax.random.fold_in(_tk, 7)
        W_top1 = 0.0606339 * jax.random.normal(jax.random.fold_in(_tk, 801), (272, 512), jnp.float32)
        W_top2 = 0.0441942 * jax.random.normal(jax.random.fold_in(_tk, 802), (512, 256), jnp.float32)
        W_top3 = 0.0625 * jax.random.normal(jax.random.fold_in(_tk, 803), (256, 1), jnp.float32)
        b_top1 = jnp.zeros((512,), jnp.float32)
        b_top2 = jnp.zeros((256,), jnp.float32)
        return (dense_ctx, ids, tbl_0, tbl_1, tbl_2, tbl_3, tbl_4, tbl_5, tbl_6, tbl_7, tbl_8, tbl_9, tbl_10, tbl_11, tbl_12, tbl_13, tbl_14, tbl_15, tbl_16, tbl_17, tbl_18, tbl_19, tbl_20, tbl_21, tbl_22, tbl_23, tbl_24, tbl_25, tbl_26, tbl_27, tbl_28, tbl_29, tbl_30, tbl_31, W_top1, b_top1, W_top2, b_top2, W_top3)
    dense_ctx, ids, tbl_0, tbl_1, tbl_2, tbl_3, tbl_4, tbl_5, tbl_6, tbl_7, tbl_8, tbl_9, tbl_10, tbl_11, tbl_12, tbl_13, tbl_14, tbl_15, tbl_16, tbl_17, tbl_18, tbl_19, tbl_20, tbl_21, tbl_22, tbl_23, tbl_24, tbl_25, tbl_26, tbl_27, tbl_28, tbl_29, tbl_30, tbl_31, W_top1, b_top1, W_top2, b_top2, W_top3 = _rec_inputs()

    def _L0_rec_setup():
        import jax, jax.numpy as jnp
        import numpy as np
        EMB_DIM = 64
        NUM_FIELDS = 32
        NUM_PAIRS = NUM_FIELDS * (NUM_FIELDS - 1) // 2
        D1 = 256
        BATCH = 256
        key = jax.random.key(seed)
        k1, k2, k3 = jax.random.split(key, 3)
        feat_emb = jax.random.normal(k1, (BATCH, NUM_FIELDS, EMB_DIM), dtype=jnp.float32)
        lim_k = float(np.sqrt(6.0 / (EMB_DIM + EMB_DIM)))
        kernel = jax.random.uniform(k2, (EMB_DIM, NUM_PAIRS, EMB_DIM), minval=-lim_k, maxval=lim_k, dtype=jnp.float32)
        lim_w = float(np.sqrt(6.0 / (NUM_PAIRS + D1)))
        W = jax.random.uniform(k3, (D1, NUM_PAIRS), minval=-lim_w, maxval=lim_w, dtype=jnp.float32)
        b = jnp.zeros((D1,), dtype=jnp.float32)
        return {'feat_emb': feat_emb, 'kernel': kernel, 'W': W, 'b': b}
    _L0_rec_all = _L0_rec_setup()
    _L0_rec_in = {k: v for k, v in _L0_rec_all.items() if k in ('kernel', 'W', 'b')}
    del _L0_rec_all
    return {'dense_ctx': dense_ctx, 'ids': ids, 'tbl_0': tbl_0, 'tbl_1': tbl_1, 'tbl_2': tbl_2, 'tbl_3': tbl_3, 'tbl_4': tbl_4, 'tbl_5': tbl_5, 'tbl_6': tbl_6, 'tbl_7': tbl_7, 'tbl_8': tbl_8, 'tbl_9': tbl_9, 'tbl_10': tbl_10, 'tbl_11': tbl_11, 'tbl_12': tbl_12, 'tbl_13': tbl_13, 'tbl_14': tbl_14, 'tbl_15': tbl_15, 'tbl_16': tbl_16, 'tbl_17': tbl_17, 'tbl_18': tbl_18, 'tbl_19': tbl_19, 'tbl_20': tbl_20, 'tbl_21': tbl_21, 'tbl_22': tbl_22, 'tbl_23': tbl_23, 'tbl_24': tbl_24, 'tbl_25': tbl_25, 'tbl_26': tbl_26, 'tbl_27': tbl_27, 'tbl_28': tbl_28, 'tbl_29': tbl_29, 'tbl_30': tbl_30, 'tbl_31': tbl_31, 'W_top1': W_top1, 'b_top1': b_top1, 'W_top2': W_top2, 'b_top2': b_top2, 'W_top3': W_top3, 'L0_rec_kernel': _L0_rec_in['kernel'], 'L0_rec_W': _L0_rec_in['W'], 'L0_rec_b': _L0_rec_in['b']}

def reference(dense_ctx, ids, tbl_0, tbl_1, tbl_2, tbl_3, tbl_4, tbl_5, tbl_6, tbl_7, tbl_8, tbl_9, tbl_10, tbl_11, tbl_12, tbl_13, tbl_14, tbl_15, tbl_16, tbl_17, tbl_18, tbl_19, tbl_20, tbl_21, tbl_22, tbl_23, tbl_24, tbl_25, tbl_26, tbl_27, tbl_28, tbl_29, tbl_30, tbl_31, W_top1, b_top1, W_top2, b_top2, W_top3, L0_rec_kernel, L0_rec_W, L0_rec_b):
    import jax
    import jax.numpy as jnp

    def _L0_rec_ref(feat_emb, kernel, W, b):
        import jax, jax.numpy as jnp
        import numpy as np
        EMB_DIM = 64
        NUM_FIELDS = 32
        NUM_PAIRS = NUM_FIELDS * (NUM_FIELDS - 1) // 2
        D1 = 256
        BATCH = 256
        num_fields = feat_emb.shape[1]
        rows, cols = np.triu_indices(num_fields, k=1)
        p = feat_emb[:, rows, :]
        q = feat_emb[:, cols, :]
        pij = jnp.einsum('bpe,dpe,bpd->bp', p, kernel, q)
        return pij @ W.T + b
    e = jnp.stack([tbl_0[ids[:, 0]], tbl_1[ids[:, 1]], tbl_2[ids[:, 2]], tbl_3[ids[:, 3]], tbl_4[ids[:, 4]], tbl_5[ids[:, 5]], tbl_6[ids[:, 6]], tbl_7[ids[:, 7]], tbl_8[ids[:, 8]], tbl_9[ids[:, 9]], tbl_10[ids[:, 10]], tbl_11[ids[:, 11]], tbl_12[ids[:, 12]], tbl_13[ids[:, 13]], tbl_14[ids[:, 14]], tbl_15[ids[:, 15]], tbl_16[ids[:, 16]], tbl_17[ids[:, 17]], tbl_18[ids[:, 18]], tbl_19[ids[:, 19]], tbl_20[ids[:, 20]], tbl_21[ids[:, 21]], tbl_22[ids[:, 22]], tbl_23[ids[:, 23]], tbl_24[ids[:, 24]], tbl_25[ids[:, 25]], tbl_26[ids[:, 26]], tbl_27[ids[:, 27]], tbl_28[ids[:, 28]], tbl_29[ids[:, 29]], tbl_30[ids[:, 30]], tbl_31[ids[:, 31]]], axis=1)
    z = _L0_rec_ref(e, L0_rec_kernel, L0_rec_W, L0_rec_b)
    z = z.reshape(z.shape[0], -1)
    h = jnp.concatenate([z, dense_ctx], axis=1)
    h = jnp.maximum(h @ W_top1 + b_top1, 0.0)
    h = jnp.maximum(h @ W_top2 + b_top2, 0.0)
    y = h @ W_top3
    return y

_drawn_inputs = setup_inputs


def setup_inputs(seed=0):
    import zlib

    import numpy as np

    out = dict(_drawn_inputs(seed))
    spreads = {'b_top1': (0.0, 0.1), 'b_top2': (0.0, 0.1), 'L0_rec_b': (0.0, 0.1)}
    factors = {'tbl_0': 3.315,
     'tbl_1': 3.028,
     'tbl_2': 3.277,
     'tbl_3': 3.129,
     'tbl_4': 3.495,
     'tbl_5': 3.306,
     'tbl_6': 3.106,
     'tbl_7': 3.179,
     'tbl_8': 3.274,
     'tbl_9': 2.909,
     'tbl_10': 3.265,
     'tbl_11': 3.041,
     'tbl_12': 3.141,
     'tbl_13': 3.235,
     'tbl_14': 3.106,
     'tbl_15': 3.204,
     'tbl_16': 3.382,
     'tbl_17': 3.158,
     'tbl_18': 3.296,
     'tbl_19': 2.921,
     'tbl_20': 3.072,
     'tbl_21': 3.363,
     'tbl_22': 3.569,
     'tbl_23': 2.911,
     'tbl_24': 3.365,
     'tbl_25': 2.944,
     'tbl_26': 3.168,
     'tbl_27': 3.373,
     'tbl_28': 3.32,
     'tbl_29': 3.346,
     'tbl_30': 3.191,
     'tbl_31': 3.218}
    for name, (base, spread) in spreads.items():
        noise = np.random.default_rng([zlib.crc32(name.encode()), seed]).standard_normal(out[name].shape)
        drawn = base * np.exp(spread * noise) if base else spread * noise
        out[name] = jnp.asarray(drawn.astype(out[name].dtype))
    for name, factor in factors.items():
        out[name] = (out[name] * factor).astype(out[name].dtype)
    return out
```

```python
from contextlib import ExitStack

import concourse.bass as bass
from concourse import mybir

NUM_FIELDS = 32
EMB = 64
BATCH = 2048
NUM_PAIRS = NUM_FIELDS * (NUM_FIELDS - 1) // 2
DENSE = 16
D1 = 256
H1 = 512
H2 = 256

P = 128
CHUNK = 512
NCHUNKS = BATCH // CHUNK
NPAIRS = NUM_FIELDS // 2
TILES = CHUNK // P

BLOCKS = [(c, j) for c in range(1, NUM_FIELDS) for j in range((c + 1) // 2)]
NBLOCKS = len(BLOCKS)
NDUOS = NBLOCKS // 2
NQUADS = NBLOCKS // 4
NGROUPS = NBLOCKS // 64
QUADS_PER_GROUP = NQUADS // NGROUPS
FIRST_BLOCK = {c: next(n for n, b in enumerate(BLOCKS) if b[0] == c) for c in range(1, NUM_FIELDS)}
LAST_BLOCK = {c: max(n for n, b in enumerate(BLOCKS) if b[0] == c) for c in range(1, NUM_FIELDS)}

PIECE = 1024
PIECES = NBLOCKS * P // PIECE
DUOS_PER_PIECE = PIECE // P // 2
K_SLOTS = 8
RAW_SLOTS = 2
M_SLOTS = 6
X_SLOTS = 3
LEAD = 4
T_DUOS = 2
TP_BANKS = 2
RED_BANKS = 2
MLP_OUTS = 9


def single(c, j):
    return 2 * j + 1 == c


def slot_pairs():
    def pair(r, c):
        return r * NUM_FIELDS - r * (r + 1) // 2 + c - r - 1

    slots = [0] * (2 * NBLOCKS)
    for n, (c, j) in enumerate(BLOCKS):
        at = (n // 64) * P + (n % 4) * 32 + 2 * ((n // 4) % 16)
        slots[at] = pair(2 * j, c)
        slots[at + 1] = slots[at] if single(c, j) else pair(2 * j + 1, c)
    return slots


def block_pairs():
    def pair(r, c):
        return r * NUM_FIELDS - r * (r + 1) // 2 + c - r - 1

    out = []
    for c, j in BLOCKS:
        out += [pair(2 * j, c), pair(2 * j if single(c, j) else 2 * j + 1, c)]
    return out


def build(nc, tables, ids, dense_t, kernel_blocks, w_slots, l0_b, w_top1, b_top1, w_top2, b_top2, w_top3, out):
    fp32 = mybir.dt.float32
    fp32r = mybir.dt.float32r
    i32 = mybir.dt.int32
    u32 = mybir.dt.uint32
    ALU = mybir.AluOpType
    ACT = mybir.ActivationFunctionType

    split_kernel = nc.dram_tensor("split_kernel", (PIECES, P, PIECE), fp32, kind="Internal").ap()

    with ExitStack() as ctx:
        def sb(name, shape, dt=fp32):
            return ctx.enter_context(nc.sbuf_tensor(name, shape, dt))

        def psum(name, shape):
            return ctx.enter_context(nc.psum_tensor(name, shape, fp32))

        def sem(name):
            return ctx.enter_context(nc.semaphore(name))

        k_ring = sb("k_ring", [P, K_SLOTS, PIECE], fp32r)
        k_raw = sb("k_raw", [EMB, RAW_SLOTS, PIECE])
        k_split = sb("k_split", [P, RAW_SLOTS, PIECE], fp32r)
        emb = sb("emb", [P, NPAIRS, TILES, 2, EMB])
        emb_t = sb("emb_t", [P, NUM_FIELDS // 2, CHUNK])
        mov = sb("mov", [P, M_SLOTS, 2, CHUNK], fp32r)
        parts = sb("parts", [P, TP_BANKS, 2, CHUNK], fp32r)
        prod = sb("prod", [P, X_SLOTS, 4, CHUNK])
        ids_sb = sb("ids_sb", [P, BATCH // P, NUM_FIELDS], i32)
        ids_now = sb("ids_now", [P, TILES, NUM_FIELDS], i32)
        ident = sb("ident", [P, P])
        pair_sel = sb("pair_sel", [P, 62])
        w_slots_sb = sb("w_slots_sb", [P, NGROUPS, D1])
        w1_sb = sb("w1_sb", [P, 2, H1])
        w1_dense_sb = sb("w1_dense_sb", [DENSE, H1])
        w2_sb = sb("w2_sb", [P, H1 // P, H2])
        w3_sb = sb("w3_sb", [P, H2 // P])
        l0_b_sb = sb("l0_b_sb", [P, D1 // P])
        b1_sb = sb("b1_sb", [P, H1 // P])
        b2_sb = sb("b2_sb", [P, H2 // P])
        dense_sb = sb("dense_sb", [DENSE, CHUNK])
        act_a = sb("act_a", [P, 4, CHUNK])
        act_b = sb("act_b", [P, 2, CHUNK])
        y_sb = sb("y_sb", [1, CHUNK])

        bilinear = psum("bilinear", [P, 2 * T_DUOS, CHUNK])
        transposed = psum("transposed", [P, TP_BANKS, CHUNK])
        pair_sums = psum("pair_sums", [P, RED_BANKS, CHUNK])

        s_ids = sem("s_ids")
        s_weights = sem("s_weights")
        s_consts = sem("s_consts")
        s_consts_pool = sem("s_consts_pool")
        s_ids_now = sem("s_ids_now")
        s_raw = [sem(f"s_raw{n}") for n in range(RAW_SLOTS)]
        s_k_hi = sem("s_k_hi")
        s_k_lo = sem("s_k_lo")
        s_k_stored = [sem(f"s_k_stored{n}") for n in range(RAW_SLOTS)]
        s_k_loaded = [sem(f"s_k_loaded{n}") for n in range(K_SLOTS)]
        s_gathered = [sem(f"s_gathered{f}") for f in range(NUM_FIELDS)]
        s_emb_open = sem("s_emb_open")
        s_transposed = sem("s_transposed")
        s_hi = sem("s_hi")
        s_lo = sem("s_lo")
        s_mov = sem("s_mov")
        s_emb_t = sem("s_emb_t")
        s_bilinear = sem("s_bilinear")
        s_prod = sem("s_prod")
        s_summed = sem("s_summed")
        s_sums_out = sem("s_sums_out")
        s_dense = sem("s_dense")
        s_mlp = sem("s_mlp")
        s_mlp_act = sem("s_mlp_act")
        s_stored = sem("s_stored")

        CREDITS = [
            (s_transposed, NPAIRS),
            (s_bilinear, DUOS_PER_PIECE * K_SLOTS),
            (s_prod, T_DUOS),
            (s_summed, X_SLOTS),
            (s_sums_out, RED_BANKS),
            (s_lo, TP_BANKS),
            (s_emb_t, TP_BANKS),
        ]
        transposed0, bilinear0, prod0, summed0, sums_out0 = (n for _, n in CREDITS[:5])
        lo0, emb_t0 = TP_BANKS, TP_BANKS

        def prepared_before(duo):
            pairs = []
            for j in range(NPAIRS):
                at = 0 if 2 * j <= LEAD else FIRST_BLOCK[2 * j - LEAD] // 2
                if at == duo:
                    pairs.append(j)
            return pairs

        block = ctx.enter_context(nc.Block())

        @block.sync
        def _(sp):
            sp.dma_start(ids_sb[:], ids.rearrange("(t p) f -> p t f", p=P)).then_inc(s_ids, 16)
            for p in range(PIECES):
                if p >= RAW_SLOTS:
                    sp.wait_ge(s_k_lo, p - RAW_SLOTS + 1)
                sp.dma_start(k_raw[:, p % RAW_SLOTS, :],
                             kernel_blocks[:, p * PIECE:(p + 1) * PIECE]).then_inc(s_raw[p % RAW_SLOTS], 16)
                if p >= 1:
                    sp.wait_ge(s_k_lo, p)
                    sp.dma_start(split_kernel[p - 1], k_split[:, (p - 1) % RAW_SLOTS, :].bitcast(fp32)).then_inc(
                        s_k_stored[(p - 1) % RAW_SLOTS], 16)
            sp.wait_ge(s_k_lo, PIECES)
            sp.dma_start(split_kernel[PIECES - 1], k_split[:, (PIECES - 1) % RAW_SLOTS, :].bitcast(fp32)).then_inc(
                s_k_stored[(PIECES - 1) % RAW_SLOTS], 16)
            with sp.Fori(0, NCHUNKS) as i:
                sp.wait_ge(s_mlp, i * MLP_OUTS)
                sp.dma_start(dense_sb[:], dense_t[:, bass.ds(i * CHUNK, CHUNK)]).then_inc(s_dense, 16)
                for p in range(PIECES):
                    sp.wait_ge(s_bilinear, i * NDUOS + DUOS_PER_PIECE * (p + 1))
                    sp.wait_ge(s_k_stored[p % RAW_SLOTS], 16 * (p // RAW_SLOTS + 1))
                    sp.dma_start(k_ring[:, p % K_SLOTS, :].bitcast(fp32), split_kernel[p]).then_inc(s_k_loaded[p % K_SLOTS], 16)
                sp.wait_ge(s_mlp_act, i * MLP_OUTS + MLP_OUTS)
                sp.dma_start(out[:, bass.ds(i * CHUNK, CHUNK)], y_sb[:]).then_inc(s_stored, 16)
            sp.wait_ge(s_stored, 16 * NCHUNKS)

        @block.gpsimd
        def _(pool):
            pool.wait_ge(s_consts, 1)
            nc.gpsimd.affine_select(out=ident[:], in_=ident[:], compare_op=ALU.not_equal, fill=1.0,
                                    base=0, pattern=[[-1, P]], channel_multiplier=1).then_inc(s_consts_pool, 1)
            pool.wait_ge(s_ids, 16)
            with pool.Fori(0, NCHUNKS) as i:
                for f in range(NUM_FIELDS):
                    pool.wait_ge(s_gathered[f], i * (16 * TILES))
                nc.gpsimd.tensor_copy(ids_now[:], ids_sb[:, bass.ds(i * TILES, TILES), :]).then_inc(s_ids_now, 1)
                pool.wait_ge(s_ids_now, i + 1)
                for f in range(NUM_FIELDS):
                    if f % 2 == 0:
                        pool.wait_ge(s_transposed, i * NPAIRS + f // 2 + 1)
                        pool.sem_inc(s_emb_open, 1)
                    for t in range(TILES):
                        nc.gpsimd.indirect_dma_start(
                            emb[:, f // 2, t, f % 2, :], None, tables[f],
                            bass.IndirectOffsetOnAxis(ap=ids_now[:, t, f:f + 1].bitcast(u32), axis=0),
                        ).then_inc(s_gathered[f], 16)

        @block.scalar
        def _(act):
            for dst, src in (
                (w_slots_sb[:], w_slots.rearrange("(g p) n -> p g n", p=P)),
                (w1_sb[:], w_top1[0:D1, :].rearrange("(g p) n -> p g n", p=P)),
                (w1_dense_sb[:], w_top1[D1:D1 + DENSE, :]),
                (w2_sb[:], w_top2.rearrange("(g p) n -> p g n", p=P)),
                (w3_sb[:], w_top3),
                (l0_b_sb[:], l0_b),
                (b1_sb[:], b_top1),
                (b2_sb[:], b_top2),
            ):
                act.dma_start(dst, src).then_inc(s_weights, 16)
            for p in range(PIECES):
                q = p % RAW_SLOTS
                act.wait_ge(s_raw[q], 16 * (p // RAW_SLOTS + 1))
                if p >= RAW_SLOTS:
                    act.wait_ge(s_k_stored[q], 16 * (p // RAW_SLOTS))
                nc.scalar.activation(k_split[0:EMB, q, :], k_raw[:, q, :], ACT.Copy).then_inc(s_k_hi, 1)
            act.wait_ge(s_weights, 16 * 8)

            with act.Fori(0, NCHUNKS) as i:
                def prepare(j):
                    act.wait_ge(s_transposed, i * NPAIRS + transposed0 + j + 1)
                    if j == 0:
                        act.wait_ge(s_prod, i * NDUOS + prod0)
                    bank = j % TP_BANKS
                    nc.scalar.activation(emb_t[:, j, :], transposed[:, bank, :], ACT.Copy).then_inc(s_emb_t, 1)
                    if j >= TP_BANKS:
                        act.wait_ge(s_mov, i * NUM_FIELDS + 2 * (j - TP_BANKS + 1))
                    else:
                        act.wait_ge(s_mov, i * NUM_FIELDS)
                    nc.scalar.activation(parts[:, bank, 0, :], transposed[:, bank, :], ACT.Copy).then_inc(s_hi, 1)
                    act.wait_ge(s_hi, i * NPAIRS + j + 1)
                    act.wait_ge(s_lo, i * NPAIRS + lo0 + j + 1)
                    for f in (2 * j, 2 * j + 1):
                        if f > M_SLOTS:
                            last = LAST_BLOCK[f - M_SLOTS] // 2
                            act.wait_ge(s_bilinear, i * NDUOS + bilinear0 + last + 1)
                        half = slice((f % 2) * EMB, (f % 2 + 1) * EMB)
                        for to in (slice(0, EMB), slice(EMB, P)):
                            ins = nc.scalar.activation(mov[to, f % M_SLOTS, :, :],
                                                       parts[half, bank, :, :].bitcast(fp32), ACT.Copy)
                        ins.then_inc(s_mov, 1)

                for duo in range(NDUOS):
                    for j in prepared_before(duo):
                        prepare(j)
                    if (duo + 1) % (2 * QUADS_PER_GROUP) == 0:
                        g = duo // (2 * QUADS_PER_GROUP)
                        if g == 0:
                            act.wait_ge(s_mlp, i * MLP_OUTS)
                        act.wait_ge(s_summed, i * NQUADS + summed0 + QUADS_PER_GROUP * (g + 1))
                        nc.scalar.activation(act_a[:, g, :], pair_sums[:, g % RED_BANKS, :],
                                             ACT.Copy).then_inc(s_sums_out, 1)

                def finish(k, dst, bias, func):
                    act.wait_ge(s_mlp, i * MLP_OUTS + k + 1)
                    rows = dst.shape[0]
                    if bias is None:
                        act.wait_ge(s_stored, i * 16)
                        ins = nc.scalar.activation(dst, bilinear[0:rows, k % 4, :], func)
                    else:
                        ins = nc.scalar.activation(dst, bilinear[0:rows, k % 4, :], func, bias=bias)
                    ins.then_inc(s_mlp_act, 1)

                for m in range(2):
                    finish(m, act_b[:, m, :], l0_b_sb[:, m:m + 1], ACT.Identity)
                for m in range(4):
                    finish(2 + m, act_a[:, m, :], b1_sb[:, m:m + 1], ACT.Relu)
                for m in range(2):
                    finish(6 + m, act_b[:, m, :], b2_sb[:, m:m + 1], ACT.Relu)
                finish(8, y_sb[:], None, ACT.Copy)

        @block.vector
        def _(dve):
            nc.vector.memset(ident[:], 0.0).then_inc(s_consts, 1)
            nc.vector.memset(pair_sel[:], 0.0).then_inc(s_consts, 1)
            dve.wait_ge(s_consts, 2)
            nc.vector.memset(pair_sel[0:EMB, 30:31], 1.0).then_inc(s_consts, 1)
            nc.vector.memset(pair_sel[EMB:P, 31:32], 1.0).then_inc(s_consts, 1)
            for s, n in CREDITS:
                dve.sem_inc(s, n)
            for p in range(PIECES):
                q = p % RAW_SLOTS
                dve.wait_ge(s_k_hi, p + 1)
                nc.vector.tensor_tensor(k_split[EMB:P, q, :], k_raw[:, q, :], k_split[0:EMB, q, :].bitcast(fp32),
                                        ALU.subtract).then_inc(s_k_lo, 1)

            with dve.Fori(0, NCHUNKS) as i:
                def prepare(j):
                    bank = j % TP_BANKS
                    dve.wait_ge(s_hi, i * NPAIRS + j + 1)
                    nc.vector.tensor_tensor(parts[:, bank, 1, :], transposed[:, bank, :],
                                            parts[:, bank, 0, :].bitcast(fp32), ALU.subtract).then_inc(s_lo, 1)

                for duo in range(NDUOS):
                    for j in prepared_before(duo):
                        prepare(j)
                    (_, j0), (c1, j1) = BLOCKS[2 * duo:2 * duo + 2]
                    if duo == 0 or BLOCKS[2 * duo - 1][0] != c1:
                        dve.wait_ge(s_emb_t, i * NPAIRS + emb_t0 + c1 // 2 + 1)
                    if duo % 2 == 0:
                        dve.wait_ge(s_summed, i * NQUADS + duo // 2 + 1)
                    dve.wait_ge(s_bilinear, i * NDUOS + bilinear0 + duo + 1)
                    other = emb_t[:, j0, :]
                    both = bass.AP(tensor=other.tensor, offset=other.offset,
                                   ap=[list(other.ap[0]), [(j1 - j0) * CHUNK, 2], [1, CHUNK]])
                    at = (duo // 2) % X_SLOTS
                    b = 2 * (duo % 2)
                    nc.vector.tensor_tensor(prod[:, at, b:b + 2, :], bilinear[:, b:b + 2, :], both,
                                            ALU.mult).then_inc(s_prod, 1)

        @block.tensor
        def _(pe):
            pe.wait_ge(s_consts, 4)
            pe.wait_ge(s_consts_pool, 1)
            pe.wait_ge(s_weights, 16 * 8)
            with pe.Fori(0, NCHUNKS) as i:
                def prepare(j):
                    pe.wait_ge(s_gathered[2 * j], (i + 1) * (16 * TILES))
                    pe.wait_ge(s_gathered[2 * j + 1], (i + 1) * (16 * TILES))
                    pe.wait_ge(s_emb_t, i * NPAIRS + j + 1)
                    pe.wait_ge(s_lo, i * NPAIRS + j + 1)
                    for t in range(TILES):
                        last = nc.tensor.transpose(transposed[:, j % TP_BANKS, t * P:(t + 1) * P],
                                                   emb[:, j, t, :, :], ident[:])
                    last.then_inc(s_transposed, 1)

                def sum_quad(quad):
                    g, pos = divmod(quad, QUADS_PER_GROUP)
                    if pos == 0:
                        pe.wait_ge(s_sums_out, i * NGROUPS + g + 1)
                    pe.wait_ge(s_prod, i * NDUOS + prod0 + 2 * quad + 2)
                    for b in sorted(range(4), key=lambda b: single(*BLOCKS[4 * quad + b])):
                        c, j = BLOCKS[4 * quad + b]
                        rows = EMB if single(c, j) else P
                        last = nc.tensor.matmul(pair_sums[32 * b:32 * b + 32, g % RED_BANKS, :],
                                                pair_sel[0:rows, 30 - 2 * pos:62 - 2 * pos],
                                                prod[0:rows, quad % X_SLOTS, b, :],
                                                start=pos == 0, stop=pos == QUADS_PER_GROUP - 1,
                                                tile_position=(0, 32 * b))
                    last.then_inc(s_summed, 1)

                pe.wait_ge(s_mlp_act, i * MLP_OUTS)
                for duo in range(NDUOS):
                    for j in prepared_before(duo):
                        prepare(j)
                    piece = duo // DUOS_PER_PIECE
                    if duo % DUOS_PER_PIECE == 0:
                        pe.wait_ge(s_k_loaded[piece % K_SLOTS],
                                   (i * (PIECES // K_SLOTS) + piece // K_SLOTS + 1) * 16)
                    pe.wait_ge(s_prod, i * NDUOS + duo + 1)
                    for n in (2 * duo, 2 * duo + 1):
                        c, j = BLOCKS[n]
                        if n == FIRST_BLOCK[c]:
                            pe.wait_ge(s_mov, i * NUM_FIELDS + c + 1)
                        col = n * P % PIECE
                        weights = k_ring[:, piece % K_SLOTS, col:col + P]
                        for part in range(2):
                            last = nc.tensor.matmul(bilinear[:, n % 4, :], weights, mov[:, c % M_SLOTS, part, :],
                                                    start=part == 0, stop=part == 1)
                    last.then_inc(s_bilinear, 1)
                    if duo % 2 == 1 and duo >= 3:
                        sum_quad(duo // 2 - 1)
                sum_quad(NQUADS - 1)

                def layer(k, terms, rows=P):
                    if k >= 4:
                        pe.wait_ge(s_mlp_act, i * MLP_OUTS + k - 3)
                    for n, (w, x) in enumerate(terms):
                        last = nc.tensor.matmul(bilinear[0:rows, k % 4, :], w, x, start=n == 0,
                                                stop=n == len(terms) - 1)
                    last.then_inc(s_mlp, 1)

                pe.wait_ge(s_sums_out, (i + 1) * NGROUPS + sums_out0)
                for m in range(2):
                    layer(m, [(w_slots_sb[:, g, m * P:(m + 1) * P], act_a[:, g, :]) for g in range(NGROUPS)])
                pe.wait_ge(s_dense, (i + 1) * 16)
                pe.wait_ge(s_mlp_act, i * MLP_OUTS + 2)
                for m in range(4):
                    cols = slice(m * P, (m + 1) * P)
                    layer(2 + m, [(w1_dense_sb[:, cols], dense_sb[:])]
                          + [(w1_sb[:, g, cols], act_b[:, g, :]) for g in range(2)])
                pe.wait_ge(s_mlp_act, i * MLP_OUTS + 6)
                for m in range(2):
                    layer(6 + m, [(w2_sb[:, g, m * P:(m + 1) * P], act_a[:, g, :]) for g in range(4)])
                pe.wait_ge(s_mlp_act, i * MLP_OUTS + 8)
                layer(8, [(w3_sb[:, g:g + 1], act_b[:, g, :]) for g in range(2)], rows=1)


def kernel(**inputs):
    import numpy as np
    import concourse.bacc as bacc
    from concourse.bass_utils import run_bass_kernel_spmd

    nc = bacc.Bacc("TRN2", target_bir_lowering=False, num_devices=1)
    arrays = {}

    def give(name, a):
        a = np.ascontiguousarray(a)
        arrays[name] = a
        return nc.dram_tensor(name, a.shape, mybir.dt.from_np(a.dtype), kind="ExternalInput").ap()

    def columns(v):
        return np.asarray(v).reshape(-1, P).T

    tables = [give(f"table_{f}", inputs[f"tbl_{f}"]) for f in range(NUM_FIELDS)]
    ids = give("ids", inputs["ids"])
    dense_t = give("dense_t", np.asarray(inputs["dense_ctx"]).T)
    k = np.asarray(inputs["L0_rec_kernel"])
    kernel_blocks = give("kernel_blocks", k[:, block_pairs(), :].reshape(EMB, NBLOCKS * P))
    w_slots = give("w_slots", np.asarray(inputs["L0_rec_W"]).T[slot_pairs()])
    l0_b = give("l0_b", columns(inputs["L0_rec_b"]))
    w_top1 = give("w_top1", inputs["W_top1"])
    b_top1 = give("b_top1", columns(inputs["b_top1"]))
    w_top2 = give("w_top2", inputs["W_top2"])
    b_top2 = give("b_top2", columns(inputs["b_top2"]))
    w_top3 = give("w_top3", columns(inputs["W_top3"]))
    out = nc.dram_tensor("out", (1, BATCH), mybir.dt.float32, kind="ExternalOutput").ap()
    build(nc, tables, ids, dense_t, kernel_blocks, w_slots, l0_b, w_top1, b_top1, w_top2, b_top2, w_top3, out)
    r = run_bass_kernel_spmd(nc, [arrays], core_ids=[0])
    return np.asarray(r.results[0]["out"]).reshape(BATCH, 1)
```

```python
from contextlib import ExitStack

import concourse.bass as bass
from concourse import mybir

NUM_FIELDS = 32
EMB = 64
BATCH = 2048
NUM_PAIRS = NUM_FIELDS * (NUM_FIELDS - 1) // 2
DENSE = 16
D1 = 256
H1 = 512
H2 = 256

P = 128
CHUNK = 512
NCHUNKS = BATCH // CHUNK
TILES = CHUNK // P
NDOUBLES = NUM_FIELDS // 2

BLOCKS = [(c, j) for c in range(1, NUM_FIELDS) for j in range((c + 1) // 2)]
NBLOCKS = len(BLOCKS)
NQUADS = NBLOCKS // 4
GROUP = 64
NGROUPS = NBLOCKS // GROUP
GROUP_QUADS = GROUP // 4
FIRST_BLOCK = {c: next(n for n, b in enumerate(BLOCKS) if b[0] == c) for c in range(1, NUM_FIELDS)}
LAST_BLOCK = {c: max(n for n, b in enumerate(BLOCKS) if b[0] == c) for c in range(1, NUM_FIELDS)}

PIECE = 1024
PIECE_BLOCKS = PIECE // P
PIECES = NBLOCKS // PIECE_BLOCKS
K_SLOTS = 4
RAW_SLOTS = 3
M_SLOTS = 8
X_SLOTS = 2
T_BANKS = 4
TP_BANKS = 2
SUM_BANKS = 2
LEAD = 4

LAYER_TERMS = [NGROUPS] * 2 + [3] * 4 + [4] * 2 + [2]
NOUTS = len(LAYER_TERMS)
Z_OUTS, H1_OUTS, H2_OUTS = 2, 6, 8


def single(c, j):
    return 2 * j + 1 == c


def slot_pairs():
    def pair(r, c):
        return r * NUM_FIELDS - r * (r + 1) // 2 + c - r - 1

    slots = [0] * (2 * NBLOCKS)
    for n, (c, j) in enumerate(BLOCKS):
        at = (n // 64) * P + (n % 4) * 32 + 2 * ((n // 4) % 16)
        slots[at] = pair(2 * j, c)
        slots[at + 1] = slots[at] if single(c, j) else pair(2 * j + 1, c)
    return slots


def block_pairs():
    def pair(r, c):
        return r * NUM_FIELDS - r * (r + 1) // 2 + c - r - 1

    out = []
    for c, j in BLOCKS:
        out += [pair(2 * j, c), pair(2 * j if single(c, j) else 2 * j + 1, c)]
    return out


def prod_slot(n):
    return n // 4 % X_SLOTS


LAYER_PHASES = [(0, 1, 2), (3, 4, 5, 6), (7, 8)]


def layer_phase(k):
    return next(g for g, outs in enumerate(LAYER_PHASES) if k in outs)


def layer_bank(k):
    return (layer_phase(k) + 1) % SUM_BANKS


def turn_steps():
    tail = FIRST_BLOCK[NUM_FIELDS - 1]
    early = {tail + 1: [("transpose", 0)], tail + 3: [("split", 0)], tail + 5: [("transpose", 1)],
             tail + 7: [("split", 1)], tail + 9: [("transpose", 2)], tail + 11: [("split", 2)]}
    ahead = {0: [("transpose", 3), ("split", 3)]}
    for j in range(4, NDOUBLES):
        n = FIRST_BLOCK[2 * j - LEAD]
        ahead.setdefault(n, []).append(("transpose", j))
        ahead.setdefault(n + 2, []).append(("split", j))
    terms = {}
    for g, outs in enumerate(LAYER_PHASES):
        quad = g * GROUP_QUADS + 2
        for k in outs:
            for term in range(LAYER_TERMS[k]):
                terms[quad] = (k, term)
                quad += 1
    steps = []
    for back, blocks in ((1, range(tail, NBLOCKS)), (0, range(tail))):
        for n in blocks:
            for kind, j in (early if back else ahead).get(n, []):
                steps.append((kind, 0, j))
            steps.append(("block", back, n))
            if n % 4 == 3:
                quad = n // 4
                steps.append(("sum", back, quad - 1) if quad else ("sum", 1, NQUADS - 1))
                if not back and quad in terms:
                    steps.append(("layer", 1, terms[quad]))
    return steps


def first_turn_steps():
    steps = [("piece", 0, p) for p in range(K_SLOTS - 1)]
    p = K_SLOTS - 1
    for kind, back, n in turn_steps():
        if back:
            continue
        if kind == "block" and p < PIECES and n == (p - K_SLOTS + 1) * PIECE_BLOCKS + 2:
            steps.append(("piece", 0, p))
            p += 1
        steps.append((kind, back, n))
    while p < PIECES:
        steps.append(("piece", 0, p))
        p += 1
    return steps


def last_turn_steps():
    return [step for step in turn_steps() if step[1]]


def run_turns(engine, turn):
    turn(0, first_turn_steps())
    with engine.Fori(1, NCHUNKS) as i:
        turn(i, turn_steps())
    turn(NCHUNKS, last_turn_steps())


def wait(engine, semaphore, count):
    if not (isinstance(count, int) and count <= 0):
        engine.wait_ge(semaphore, count)


def build(nc, tables, ids, dense_t, kernel_blocks, w_slots, l0_b, w_top1, b_top1, w_top2, b_top2, w_top3, out):
    fp32 = mybir.dt.float32
    fp32r = mybir.dt.float32r
    i32 = mybir.dt.int32
    u32 = mybir.dt.uint32
    ALU = mybir.AluOpType
    ACT = mybir.ActivationFunctionType

    split_kernel = nc.dram_tensor("split_kernel", (PIECES, P, PIECE), fp32, kind="Internal").ap()

    with ExitStack() as ctx:
        def sb(name, shape, dt=fp32):
            return ctx.enter_context(nc.sbuf_tensor(name, shape, dt))

        def psum(name, shape):
            return ctx.enter_context(nc.psum_tensor(name, shape, fp32))

        def sem(name):
            return ctx.enter_context(nc.semaphore(name))

        k_ring = sb("k_ring", [P, K_SLOTS, PIECE], fp32r)
        k_raw = sb("k_raw", [EMB, RAW_SLOTS, PIECE])
        emb = sb("emb", [P, NDOUBLES, TILES, 2, EMB])
        emb_t = sb("emb_t", [P, NDOUBLES, CHUNK])
        parts = sb("parts", [P, TP_BANKS, 2, CHUNK], fp32r)
        mov = sb("mov", [P, M_SLOTS, 2, CHUNK], fp32r)
        prod = sb("prod", [P, X_SLOTS, 4, CHUNK])
        ids_sb = sb("ids_sb", [P, BATCH // P, NUM_FIELDS], i32)
        ids_now = sb("ids_now", [P, TILES, NUM_FIELDS], i32)
        ident = sb("ident", [P, P])
        pair_sel = sb("pair_sel", [P, 62])
        w_slots_sb = sb("w_slots_sb", [P, NGROUPS, D1])
        w1_sb = sb("w1_sb", [P, 2, H1])
        w1_dense_sb = sb("w1_dense_sb", [DENSE, H1])
        w2_sb = sb("w2_sb", [P, H1 // P, H2])
        w3_sb = sb("w3_sb", [P, H2 // P])
        l0_b_sb = sb("l0_b_sb", [P, D1 // P])
        b1_sb = sb("b1_sb", [P, H1 // P])
        b2_sb = sb("b2_sb", [P, H2 // P])
        dense_sb = sb("dense_sb", [DENSE, CHUNK])
        sums_sb = sb("sums_sb", [P, NGROUPS, CHUNK])
        h1_sb = sb("h1_sb", [P, H1 // P, CHUNK])
        zh2_sb = sb("zh2_sb", [P, 2, CHUNK])
        y_sb = sb("y_sb", [1, BATCH])

        bilinear = psum("bilinear", [P, T_BANKS, CHUNK])
        transposed = psum("transposed", [P, TP_BANKS, CHUNK])
        sums = psum("sums", [P, SUM_BANKS, CHUNK])

        s_ids = sem("s_ids")
        s_weights = sem("s_weights")
        s_consts = sem("s_consts")
        s_ident = sem("s_ident")
        s_ids_now = sem("s_ids_now")
        s_raw = [sem(f"s_raw{n}") for n in range(RAW_SLOTS)]
        s_k_hi = sem("s_k_hi")
        s_k_lo = sem("s_k_lo")
        s_k_stored = [sem(f"s_k_stored{n}") for n in range(K_SLOTS)]
        s_k_loaded = [sem(f"s_k_loaded{n}") for n in range(K_SLOTS)]
        s_gathered = [sem(f"s_gathered{f}") for f in range(NUM_FIELDS)]
        s_emb_open = sem("s_emb_open")
        s_transposed = sem("s_transposed")
        s_emb_t = sem("s_emb_t")
        s_hi = sem("s_hi")
        s_lo = sem("s_lo")
        s_mov = sem("s_mov")
        s_bilinear = sem("s_bilinear")
        s_prod = sem("s_prod")
        s_summed = sem("s_summed")
        s_sums_out = sem("s_sums_out")
        s_dense = sem("s_dense")
        s_layer = sem("s_layer")
        s_layer_out = sem("s_layer_out")
        s_stored = sem("s_stored")

        NMOV = NUM_FIELDS - 1

        block = ctx.enter_context(nc.Block())

        @block.sync
        def _(sp):
            sp.dma_start(ids_sb[:], ids.rearrange("(t p) f -> p t f", p=P)).then_inc(s_ids, 16)
            for p in range(PIECES + RAW_SLOTS):
                if p < PIECES:
                    wait(sp, s_k_lo, p - RAW_SLOTS + 1)
                    sp.dma_start(k_raw[:, p % RAW_SLOTS, :],
                                 kernel_blocks[:, p * PIECE:(p + 1) * PIECE]).then_inc(s_raw[p % RAW_SLOTS], 16)
                q = p - RAW_SLOTS
                if q >= 0:
                    sp.wait_ge(s_k_lo, q + 1)
                    sp.dma_start(split_kernel[q], k_ring[:, q % K_SLOTS, :].bitcast(fp32)).then_inc(
                        s_k_stored[q % K_SLOTS], 16)
            sp.dma_start(dense_sb[:], dense_t[:, 0:CHUNK]).then_inc(s_dense, 16)
            with sp.Fori(1, NCHUNKS) as i:
                for p in range(PIECES):
                    sp.wait_ge(s_bilinear, i * NBLOCKS + PIECE_BLOCKS * (p - K_SLOTS + 1))
                    sp.wait_ge(s_k_stored[p % K_SLOTS], 16 * (PIECES // K_SLOTS))
                    sp.dma_start(k_ring[:, p % K_SLOTS, :].bitcast(fp32), split_kernel[p]).then_inc(
                        s_k_loaded[p % K_SLOTS], 16)
                sp.wait_ge(s_layer, (i - 1) * NOUTS + H1_OUTS)
                sp.dma_start(dense_sb[:], dense_t[:, bass.ds(i * CHUNK, CHUNK)]).then_inc(s_dense, 16)
            sp.wait_ge(s_layer_out, NCHUNKS * NOUTS)
            sp.dma_start(out, y_sb[:]).then_inc(s_stored, 16)
            sp.wait_ge(s_stored, 16)

        @block.gpsimd
        def _(pool):
            pool.wait_ge(s_consts, 1)
            nc.gpsimd.affine_select(out=ident[:], in_=ident[:], compare_op=ALU.not_equal, fill=1.0,
                                    base=0, pattern=[[-1, P]], channel_multiplier=1).then_inc(s_ident, 1)
            pool.wait_ge(s_ids, 16)

            def gather_chunk(i):
                for f in range(NUM_FIELDS):
                    wait(pool, s_gathered[f], i * (16 * TILES))
                nc.gpsimd.tensor_copy(ids_now[:], ids_sb[:, bass.ds(i * TILES, TILES), :]).then_inc(s_ids_now, 1)
                pool.wait_ge(s_ids_now, i + 1)
                for f in range(NUM_FIELDS):
                    if f % 2 == 0:
                        wait(pool, s_transposed, (i - 1) * NDOUBLES + f // 2 + 1)
                        pool.sem_inc(s_emb_open, 1)
                    for t in range(TILES):
                        nc.gpsimd.indirect_dma_start(
                            emb[:, f // 2, t, f % 2, :], None, tables[f],
                            bass.IndirectOffsetOnAxis(ap=ids_now[:, t, f:f + 1].bitcast(u32), axis=0),
                        ).then_inc(s_gathered[f], 16)

            gather_chunk(0)
            with pool.Fori(1, NCHUNKS) as i:
                gather_chunk(i)

        @block.scalar
        def _(act):
            weights = (
                (w_slots_sb[:], w_slots.rearrange("(g p) n -> p g n", p=P)),
                (w1_sb[:], w_top1[0:D1, :].rearrange("(g p) n -> p g n", p=P)),
                (w1_dense_sb[:], w_top1[D1:D1 + DENSE, :]),
                (w2_sb[:], w_top2.rearrange("(g p) n -> p g n", p=P)),
                (w3_sb[:], w_top3),
                (l0_b_sb[:], l0_b),
                (b1_sb[:], b_top1),
                (b2_sb[:], b_top2),
            )
            for dst, src in weights:
                act.dma_start(dst, src).then_inc(s_weights, 16)
            act.wait_ge(s_weights, 16 * len(weights))

            def split_piece(p):
                slot = p % K_SLOTS
                act.wait_ge(s_raw[p % RAW_SLOTS], 16 * (p // RAW_SLOTS + 1))
                wait(act, s_bilinear, PIECE_BLOCKS * (p - K_SLOTS + 1))
                wait(act, s_k_stored[slot], 16 * (p // K_SLOTS))
                nc.scalar.activation(k_ring[0:EMB, slot, :], k_raw[:, p % RAW_SLOTS, :],
                                     ACT.Copy).then_inc(s_k_hi, 1)

            def transposed_out(i, j):
                bank = j % TP_BANKS
                act.wait_ge(s_transposed, i * NDOUBLES + j + 1)
                wait(act, s_mov, i * NMOV + 2 * (j - TP_BANKS) + 1)
                nc.scalar.activation(parts[:, bank, 0, :], transposed[:, bank, :], ACT.Copy).then_inc(s_hi, 1)
                wait(act, s_prod, (i - 1) * NBLOCKS + FIRST_BLOCK[NUM_FIELDS - 1] + j + 1)
                nc.scalar.activation(emb_t[:, j, :], transposed[:, bank, :], ACT.Copy).then_inc(s_emb_t, 1)

            def spread(i, j):
                bank = j % TP_BANKS
                act.wait_ge(s_hi, i * NDOUBLES + j + 1)
                act.wait_ge(s_lo, i * NDOUBLES + j + 1)
                for f in (2 * j, 2 * j + 1):
                    if f == 0:
                        continue
                    if f > M_SLOTS:
                        act.wait_ge(s_bilinear, i * NBLOCKS + LAST_BLOCK[f - M_SLOTS] + 1)
                    else:
                        old = f - M_SLOTS + NUM_FIELDS
                        wait(act, s_bilinear, (i - 1) * NBLOCKS + LAST_BLOCK.get(old, -1) + 1)
                    half = slice((f % 2) * EMB, (f % 2 + 1) * EMB)
                    nc.scalar.activation(mov[0:EMB, f % M_SLOTS, :, :], parts[half, bank, :, :].bitcast(fp32),
                                         ACT.Copy)
                    nc.scalar.activation(mov[EMB:P, f % M_SLOTS, :, :], parts[half, bank, :, :].bitcast(fp32),
                                         ACT.Copy).then_inc(s_mov, 1)

            def group_out(i, g):
                act.wait_ge(s_summed, i * NQUADS + GROUP_QUADS * (g + 1))
                if g == 0:
                    wait(act, s_layer, (i - 1) * NOUTS + Z_OUTS)
                nc.scalar.activation(sums_sb[:, g, :], sums[:, g % SUM_BANKS, :], ACT.Copy).then_inc(s_sums_out, 1)

            def layer_out(i, k):
                act.wait_ge(s_layer, i * NOUTS + k + 1)
                source = sums[:, layer_bank(k), :]
                if k < Z_OUTS:
                    nc.scalar.activation(zh2_sb[:, k, :], source, ACT.Identity,
                                         bias=l0_b_sb[:, k:k + 1]).then_inc(s_layer_out, 1)
                elif k < H1_OUTS:
                    m = k - Z_OUTS
                    nc.scalar.activation(h1_sb[:, m, :], source, ACT.Relu,
                                         bias=b1_sb[:, m:m + 1]).then_inc(s_layer_out, 1)
                elif k < H2_OUTS:
                    m = k - H1_OUTS
                    nc.scalar.activation(zh2_sb[:, m, :], source, ACT.Relu,
                                         bias=b2_sb[:, m:m + 1]).then_inc(s_layer_out, 1)
                else:
                    nc.scalar.activation(y_sb[:, bass.ds(i * CHUNK, CHUNK)], source[0:1, :],
                                         ACT.Copy).then_inc(s_layer_out, 1)

            def turn(now, steps):
                for kind, back, n in steps:
                    i = now - back
                    if kind == "piece":
                        split_piece(n)
                    elif kind == "transpose":
                        transposed_out(i, n)
                    elif kind == "split":
                        spread(i, n)
                    elif kind == "sum" and (n + 1) % GROUP_QUADS == 0:
                        group_out(i, n // GROUP_QUADS)
                    elif kind == "layer" and n[1] == LAYER_TERMS[n[0]] - 1:
                        layer_out(i, n[0])

            run_turns(act, turn)

        @block.vector
        def _(dve):
            nc.vector.memset(ident[:], 0.0).then_inc(s_consts, 1)
            nc.vector.memset(pair_sel[:], 0.0).then_inc(s_consts, 1)
            dve.wait_ge(s_consts, 2)
            nc.vector.memset(pair_sel[0:EMB, 30:31], 1.0).then_inc(s_consts, 1)
            nc.vector.memset(pair_sel[EMB:P, 31:32], 1.0).then_inc(s_consts, 1)

            def split_piece(p):
                slot = p % K_SLOTS
                dve.wait_ge(s_k_hi, p + 1)
                nc.vector.tensor_tensor(k_ring[EMB:P, slot, :], k_raw[:, p % RAW_SLOTS, :],
                                        k_ring[0:EMB, slot, :].bitcast(fp32), ALU.subtract).then_inc(s_k_lo, 1)

            def split_double(i, j):
                bank = j % TP_BANKS
                dve.wait_ge(s_hi, i * NDOUBLES + j + 1)
                dve.wait_ge(s_emb_t, i * NDOUBLES + j + 1)
                nc.vector.tensor_tensor(parts[:, bank, 1, :], emb_t[:, j, :],
                                        parts[:, bank, 0, :].bitcast(fp32), ALU.subtract).then_inc(s_lo, 1)

            def multiply(i, n):
                c, j = BLOCKS[n]
                if n == FIRST_BLOCK[c]:
                    dve.wait_ge(s_emb_t, i * NDOUBLES + c // 2 + 1)
                if n % 4 == 0:
                    wait(dve, s_summed, i * NQUADS + n // 4 - X_SLOTS + 1)
                dve.wait_ge(s_bilinear, i * NBLOCKS + n + 1)
                nc.vector.tensor_tensor(prod[:, prod_slot(n), n % 4, :], bilinear[:, n % T_BANKS, :],
                                        emb_t[:, j, :], ALU.mult).then_inc(s_prod, 1)

            def turn(now, steps):
                for kind, back, n in steps:
                    i = now - back
                    if kind == "piece":
                        split_piece(n)
                    elif kind == "split":
                        split_double(i, n)
                    elif kind == "block":
                        multiply(i, n)

            run_turns(dve, turn)

        @block.tensor
        def _(pe):
            pe.wait_ge(s_consts, 4)
            pe.wait_ge(s_ident, 1)
            pe.wait_ge(s_weights, 16 * 8)

            def transpose_double(i, j):
                pe.wait_ge(s_gathered[2 * j], (i + 1) * (16 * TILES))
                pe.wait_ge(s_gathered[2 * j + 1], (i + 1) * (16 * TILES))
                wait(pe, s_emb_t, i * NDOUBLES + j - TP_BANKS + 1)
                for t in range(TILES):
                    last = nc.tensor.transpose(transposed[:, j % TP_BANKS, t * P:(t + 1) * P],
                                               emb[:, j, t, :, :], ident[:])
                last.then_inc(s_transposed, 1)

            def bilinear_block(now, i, n):
                c, j = BLOCKS[n]
                piece = n // PIECE_BLOCKS
                slot = piece % K_SLOTS
                if n % PIECE_BLOCKS == 0 or n == FIRST_BLOCK[NUM_FIELDS - 1]:
                    if isinstance(i, int) and i == 0:
                        pe.wait_ge(s_k_lo, piece + 1)
                    else:
                        pe.wait_ge(s_k_loaded[slot], ((i - 1) * (PIECES // K_SLOTS) + piece // K_SLOTS + 1) * 16)
                if n == FIRST_BLOCK[c]:
                    pe.wait_ge(s_mov, i * NMOV + c)
                wait(pe, s_prod, i * NBLOCKS + n - T_BANKS + 1)
                col = n % PIECE_BLOCKS * P
                for part in range(2):
                    last = nc.tensor.matmul(bilinear[:, n % T_BANKS, :], k_ring[:, slot, col:col + P],
                                            mov[:, c % M_SLOTS, part, :], start=part == 0, stop=part == 1)
                last.then_inc(s_bilinear, 1)

            def sum_quad(i, quad):
                g, pos = divmod(quad, GROUP_QUADS)
                if pos == 0:
                    wait(pe, s_sums_out, i * NGROUPS + g - SUM_BANKS + 1)
                    outs = sum(layer_phase(k) < g for k in range(NOUTS))
                    wait(pe, s_layer_out, (i - 1) * NOUTS + outs)
                pe.wait_ge(s_prod, i * NBLOCKS + 4 * quad + 4)
                for b in sorted(range(4), key=lambda b: single(*BLOCKS[4 * quad + b])):
                    rows = EMB if single(*BLOCKS[4 * quad + b]) else P
                    last = nc.tensor.matmul(sums[32 * b:32 * b + 32, g % SUM_BANKS, :],
                                            pair_sel[0:rows, 30 - 2 * pos:62 - 2 * pos],
                                            prod[0:rows, prod_slot(4 * quad), b, :],
                                            start=pos == 0, stop=pos == GROUP_QUADS - 1,
                                            tile_position=(0, 32 * b))
                last.then_inc(s_summed, 1)

            def layer(i, k, term):
                last_term = term == LAYER_TERMS[k] - 1
                if term == 0:
                    meanwhile = 0 if isinstance(i, int) else layer_phase(k)
                    pe.wait_ge(s_sums_out, (i + 1) * NGROUPS + meanwhile)
                    if k:
                        pe.wait_ge(s_layer_out, i * NOUTS + k)
                if k < Z_OUTS:
                    weights, x = w_slots_sb[:, term, k * P:(k + 1) * P], sums_sb[:, term, :]
                elif k < H1_OUTS:
                    cols = slice((k - Z_OUTS) * P, (k - Z_OUTS + 1) * P)
                    if term == 0:
                        pe.wait_ge(s_dense, (i + 1) * 16)
                        weights, x = w1_dense_sb[:, cols], dense_sb[:]
                    else:
                        weights, x = w1_sb[:, term - 1, cols], zh2_sb[:, term - 1, :]
                elif k < H2_OUTS:
                    weights, x = w2_sb[:, term, (k - H1_OUTS) * P:(k - H1_OUTS + 1) * P], h1_sb[:, term, :]
                else:
                    weights, x = w3_sb[:, term:term + 1], zh2_sb[:, term, :]
                last = nc.tensor.matmul(sums[0:weights.shape[1], layer_bank(k), :], weights, x,
                                        start=term == 0, stop=last_term)
                if last_term:
                    last.then_inc(s_layer, 1)

            def turn(now, steps):
                for kind, back, n in steps:
                    i = now - back
                    if kind == "transpose":
                        transpose_double(i, n)
                    elif kind == "block":
                        bilinear_block(now, i, n)
                    elif kind == "sum":
                        sum_quad(i, n)
                    elif kind == "layer":
                        layer(i, *n)

            run_turns(pe, turn)


def kernel(**inputs):
    import numpy as np
    import concourse.bacc as bacc
    from concourse.bass_utils import run_bass_kernel_spmd

    nc = bacc.Bacc("TRN2", target_bir_lowering=False, num_devices=1)
    arrays = {}

    def give(name, a):
        a = np.ascontiguousarray(a)
        arrays[name] = a
        return nc.dram_tensor(name, a.shape, mybir.dt.from_np(a.dtype), kind="ExternalInput").ap()

    def columns(v):
        return np.asarray(v).reshape(-1, P).T

    tables = [give(f"table_{f}", inputs[f"tbl_{f}"]) for f in range(NUM_FIELDS)]
    ids = give("ids", inputs["ids"])
    dense_t = give("dense_t", np.asarray(inputs["dense_ctx"]).T)
    k = np.asarray(inputs["L0_rec_kernel"])
    kernel_blocks = give("kernel_blocks", k[:, block_pairs(), :].reshape(EMB, NBLOCKS * P))
    w_slots = give("w_slots", np.asarray(inputs["L0_rec_W"]).T[slot_pairs()])
    l0_b = give("l0_b", columns(inputs["L0_rec_b"]))
    w_top1 = give("w_top1", inputs["W_top1"])
    b_top1 = give("b_top1", columns(inputs["b_top1"]))
    w_top2 = give("w_top2", inputs["W_top2"])
    b_top2 = give("b_top2", columns(inputs["b_top2"]))
    w_top3 = give("w_top3", columns(inputs["W_top3"]))
    out = nc.dram_tensor("out", (1, BATCH), mybir.dt.float32, kind="ExternalOutput").ap()
    build(nc, tables, ids, dense_t, kernel_blocks, w_slots, l0_b, w_top1, b_top1, w_top2, b_top2, w_top3, out)
    r = run_bass_kernel_spmd(nc, [arrays], core_ids=[0])
    return np.asarray(r.results[0]["out"]).reshape(BATCH, 1)
```

```python
from contextlib import ExitStack

import concourse.bass as bass
from concourse import mybir

NUM_FIELDS = 32
EMB = 64
BATCH = 2048
NUM_PAIRS = NUM_FIELDS * (NUM_FIELDS - 1) // 2
DENSE = 16
D1 = 256
H1 = 512
H2 = 256

P = 128
CHUNK = 512
NCHUNKS = BATCH // CHUNK
TILES = CHUNK // P
NDOUBLES = NUM_FIELDS // 2

BLOCKS = []
for _c in range(2, NUM_FIELDS):
    BLOCKS += [(_c, _j) for _j in range(_c // 2)]
    if _c % 4 == 2:
        BLOCKS.append((_c, None))
NBLOCKS = len(BLOCKS)
NQUADS = NBLOCKS // 4
GROUP = 64
NGROUPS = -(-NBLOCKS // GROUP)
GROUP_QUADS = GROUP // 4
FIRST_BLOCK = {c: BLOCKS.index((c, 0)) for c in range(2, NUM_FIELDS)}
LAST_BLOCK = {c: max(n for n, b in enumerate(BLOCKS) if b[0] == c or b == (c + 1, None))
              for c in range(1, NUM_FIELDS)}

PIECE = 1024
PIECE_BLOCKS = PIECE // P
K_SLOTS = 8
K_LOADS = 4
SPLIT_AHEAD = 5
PLACES = [n for n, b in enumerate(BLOCKS) for _ in range(2 if b[1] is None else 1)]
PIECES = len(PLACES) // PIECE_BLOCKS
assert PIECES * PIECE_BLOCKS == len(PLACES) and PIECES % K_SLOTS == 0
RAW_SLOTS = 3
M_SLOTS = 8
X_SLOTS = 2
T_BANKS = 4
TP_BANKS = 2
SUM_BANKS = 2
assert NBLOCKS % (4 * X_SLOTS) == 0 and NBLOCKS % T_BANKS == 0
LEAD = 4
GPSIMD_PIECES = tuple(range(11, 28))

SPARE_AT = 2 * (NQUADS - (NGROUPS - 1) * GROUP_QUADS)
SPARE = 32 - SPARE_AT
assert 4 * SPARE == DENSE

LAYER_TERMS = [NGROUPS] * 4 + [4] * 2 + [2]
NOUTS = len(LAYER_TERMS)
H1_OUTS, H2_OUTS = 4, 6


def places_of(n):
    return [place for place, block in enumerate(PLACES) if block == n]


def piece_done(p):
    chunk, piece = divmod(p, PIECES)
    return chunk * NBLOCKS + PLACES[(piece + 1) * PIECE_BLOCKS - 1] + 1


def pair_index(r, c):
    return r * NUM_FIELDS - r * (r + 1) // 2 + c - r - 1


def block_pairs(n):
    c, j = BLOCKS[n]
    if j is None:
        return (c - 2, c - 1), (c, c + 1)
    return (2 * j, c), (2 * j + 1, c)


def slot_pairs():
    slots = [0] * (NGROUPS * P)
    for n in range(NBLOCKS):
        at = n // GROUP * P + n % 4 * 32 + 2 * (n // 4 % GROUP_QUADS)
        slots[at:at + 2] = [pair_index(*pair) for pair in block_pairs(n)]
    return slots


def gpsimd_piece_after(f):
    piece = f - 9
    if f == NUM_FIELDS - 1:
        return [p for p in GPSIMD_PIECES if p >= piece]
    return [piece] if piece in GPSIMD_PIECES else []


def prod_slot(n):
    return n // 4 % X_SLOTS


LAYER_PHASES = [(0, 1, 2, 3), (4, 5, 6)]


def layer_phase(k):
    return next(g for g, outs in enumerate(LAYER_PHASES) if k in outs)


def layer_bank(k):
    return (layer_phase(k) + 1) % SUM_BANKS


def turn_steps():
    tail = FIRST_BLOCK[NUM_FIELDS - 1]
    early = {tail + 1: [("transpose", 0)], tail + 3: [("split", 0)],
             tail + 4: [("transpose", 1)], tail + 6: [("split", 1)],
             tail + 8: [("transpose", 2)], tail + 11: [("split", 2)]}
    ahead = {0: [("transpose", 3)], 1: [("split", 3)]}
    for j in range(4, NDOUBLES):
        n = FIRST_BLOCK[2 * j - LEAD]
        ahead.setdefault(n, []).append(("transpose", j))
        ahead.setdefault(n + 3, []).append(("split", j))
    terms = {}
    for g, outs in enumerate(LAYER_PHASES):
        products = [(k, term) for k in outs for term in range(LAYER_TERMS[k])]
        for at, product in enumerate(products):
            quad = g * GROUP_QUADS + 2 + (at // 2 if g == 0 else at)
            terms.setdefault(quad, []).append(product)
    steps = []
    for back, blocks in ((1, range(tail, NBLOCKS)), (0, range(tail))):
        for n in blocks:
            for kind, j in (early if back else ahead).get(n, []):
                steps.append((kind, 0, j))
            steps.append(("block", back, n))
            if n % 4 == 3:
                quad = n // 4
                steps.append(("sum", back, quad - 1) if quad else ("sum", 1, NQUADS - 1))
                if not back:
                    steps += [("layer", 1, product) for product in terms.get(quad, [])]
    return steps


def first_turn_steps():
    ahead = {}
    for p in range(SPLIT_AHEAD):
        ahead.setdefault(0, []).extend([("piece_hi", 0, p), ("piece_lo", 0, p)])
    ahead[0] += [("transpose", 0, 0), ("split", 0, 0), ("transpose", 0, 1), ("split", 0, 1)]
    for j in range(2, NDOUBLES):
        at, end = FIRST_BLOCK[2 * j - 2], FIRST_BLOCK[2 * j]
        ahead.setdefault(min(at, end), []).append(("transpose", 0, j))
        ahead.setdefault(min(at + 2, end), []).append(("split", 0, j))
    for p in range(SPLIT_AHEAD, PIECES):
        n = piece_done(p - SPLIT_AHEAD)
        ahead.setdefault(n + 1, []).append(("piece_hi", 0, p))
        ahead.setdefault(n + 7, []).append(("piece_lo", 0, p))
    steps = []
    for step in turn_steps():
        kind, back, n = step
        if back or kind in ("transpose", "split"):
            continue
        if kind == "block":
            steps += ahead.pop(n, [])
        steps.append(step)
    assert not ahead
    return steps


def last_turn_steps():
    return [step for step in turn_steps() if step[1]]


def run_turns(engine, turn):
    turn(0, first_turn_steps())
    with engine.Fori(1, NCHUNKS) as i:
        turn(i, turn_steps())
    turn(NCHUNKS, last_turn_steps())


def wait(engine, semaphore, count):
    if not (isinstance(count, int) and count <= 0):
        engine.wait_ge(semaphore, count)


def build(nc, tables, ids, dense_t, kernel_blocks, w_cols, l0_b, w_top1, b_top1, w_top2, b_top2, w_top3, out):
    fp32 = mybir.dt.float32
    fp32r = mybir.dt.float32r
    i32 = mybir.dt.int32
    u32 = mybir.dt.uint32
    ALU = mybir.AluOpType
    ACT = mybir.ActivationFunctionType

    split_kernel = nc.dram_tensor("split_kernel", (PIECES, P, PIECE), fp32, kind="Internal").ap()

    with ExitStack() as ctx:
        def sb(name, shape, dt=fp32):
            return ctx.enter_context(nc.sbuf_tensor(name, shape, dt))

        def psum(name, shape):
            return ctx.enter_context(nc.psum_tensor(name, shape, fp32))

        def sem(name):
            return ctx.enter_context(nc.semaphore(name))

        k_ring = sb("k_ring", [P, K_SLOTS, PIECE], fp32r)
        k_raw = sb("k_raw", [EMB, RAW_SLOTS, PIECE])
        emb = sb("emb", [P, NDOUBLES, TILES, 2, EMB])
        emb_t = sb("emb_t", [P, NDOUBLES, CHUNK])
        parts = sb("parts", [P, TP_BANKS, 2, CHUNK], fp32r)
        mov = sb("mov", [P, M_SLOTS, 2, CHUNK], fp32r)
        prod = sb("prod", [P, X_SLOTS, 4, CHUNK])
        ids_sb = sb("ids_sb", [P, BATCH // P, NUM_FIELDS], i32)
        ids_now = sb("ids_now", [P, TILES, NUM_FIELDS], i32)
        ident = sb("ident", [P, P])
        pair_sel = sb("pair_sel", [P, 62])
        w_comb_sb = sb("w_comb_sb", [P, NGROUPS, H1])
        b_comb_sb = sb("b_comb_sb", [P, H1 // P])
        w2_sb = sb("w2_sb", [P, H1 // P, H2])
        w3_sb = sb("w3_sb", [P, H2 // P])
        l0_b_sb = sb("l0_b_sb", [P, D1 // P])
        b1_sb = sb("b1_sb", [P, H1 // P])
        b2_sb = sb("b2_sb", [P, H2 // P])
        sums_sb = sb("sums_sb", [P, NGROUPS, CHUNK])
        h1_sb = sb("h1_sb", [P, H1 // P, CHUNK])
        h2_sb = sb("h2_sb", [P, H2 // P, CHUNK])
        w_cols_sb, w1_sb = h1_sb[:, 0:D1 // P, :], h1_sb[:, D1 // P:, :]
        y_sb = sb("y_sb", [1, BATCH])

        bilinear = psum("bilinear", [P, T_BANKS, CHUNK])
        transposed = psum("transposed", [P, TP_BANKS, CHUNK])
        sums = psum("sums", [P, SUM_BANKS, CHUNK])

        s_ids = sem("s_ids")
        s_factors = sem("s_factors")
        s_folded = sem("s_folded")
        s_folded_out = sem("s_folded_out")
        s_weights = sem("s_weights")
        s_consts = sem("s_consts")
        s_ident = sem("s_ident")
        s_ids_now = sem("s_ids_now")
        s_raw = [sem(f"s_raw{n}") for n in range(RAW_SLOTS)]
        s_k_hi = sem("s_k_hi")
        s_k_lo = sem("s_k_lo")
        s_k_lo_gps = sem("s_k_lo_gps")
        s_k_stored = [sem(f"s_k_stored{n}") for n in range(K_SLOTS)]
        s_k_loaded = [sem(f"s_k_loaded{n}") for n in range(K_SLOTS)]
        s_gathered = [sem(f"s_gathered{f}") for f in range(NUM_FIELDS)]
        s_emb_open = sem("s_emb_open")
        s_transposed = sem("s_transposed")
        s_emb_t = sem("s_emb_t")
        s_hi = sem("s_hi")
        s_lo = sem("s_lo")
        s_spread_open = sem("s_spread_open")
        s_mov = sem("s_mov")
        s_mov_far = [sem(f"s_mov_far{n}") for n in range(M_SLOTS)]
        s_bilinear = sem("s_bilinear")
        s_prod = sem("s_prod")
        s_summed = sem("s_summed")
        s_sums_out = sem("s_sums_out")
        s_dense_open = sem("s_dense_open")
        s_dense = sem("s_dense")
        s_layer = sem("s_layer")
        s_layer_out = sem("s_layer_out")
        s_stored = sem("s_stored")

        NMOV = NUM_FIELDS - 1

        def layer_target(i, k):
            return bilinear[:, k % T_BANKS, :] if isinstance(i, int) else sums[:, layer_bank(k), :]

        def k_split(p):
            mine = p in GPSIMD_PIECES
            count = sum((x in GPSIMD_PIECES) == mine for x in range(p + 1))
            return s_k_lo_gps if mine else s_k_lo, count

        def halves(f):
            low, high = slice(0, EMB), slice(EMB, P)
            return (high, low) if f % 2 else (low, high)

        def mov_open(i, f):
            if f > M_SLOTS:
                return s_bilinear, i * NBLOCKS + LAST_BLOCK[f - M_SLOTS] + 1
            return s_bilinear, (i - 1) * NBLOCKS + LAST_BLOCK.get(f - M_SLOTS + NUM_FIELDS, -1) + 1

        def mov_far_count(i, f):
            fields = [x for x in range(1, NUM_FIELDS) if x % M_SLOTS == f % M_SLOTS]
            return 16 * (i * len(fields) + fields.index(f) + 1)

        block = ctx.enter_context(nc.Block())

        @block.sync
        def _(sp):
            sp.dma_start(ids_sb[:], ids.rearrange("(t p) f -> p t f", p=P)).then_inc(s_ids, 16)

            def load_raw(p):
                if p >= RAW_SLOTS:
                    sp.wait_ge(*k_split(p - RAW_SLOTS))
                sp.dma_start(k_raw[:, p % RAW_SLOTS, :],
                             kernel_blocks[:, p * PIECE:(p + 1) * PIECE]).then_inc(s_raw[p % RAW_SLOTS], 16)

            def store_split(p):
                sp.wait_ge(*k_split(p))
                sp.dma_start(split_kernel[p], k_ring[:, p % K_SLOTS, :].bitcast(fp32)).then_inc(
                    s_k_stored[p % K_SLOTS], 16)

            def load_split(i, p):
                sp.wait_ge(s_bilinear, i * NBLOCKS + piece_done(p - K_SLOTS))
                sp.wait_ge(s_k_stored[p % K_SLOTS], 16 * (PIECES // K_SLOTS))
                sp.dma_start(k_ring[:, p % K_SLOTS, :].bitcast(fp32), split_kernel[p]).then_inc(
                    s_k_loaded[p % K_SLOTS], 16)

            def spread_far(i, j):
                sp.wait_ge(s_lo, i * NDOUBLES + j + 1)
                sp.sem_inc(s_spread_open, 1)
                for f in (2 * j, 2 * j + 1):
                    if f == 0:
                        continue
                    wait(sp, *mov_open(i, f))
                    near, far = halves(f)
                    sp.dma_start(mov[far, f % M_SLOTS, :, :].bitcast(fp32),
                                 parts[near, j % TP_BANKS, :, :].bitcast(fp32)).then_inc(s_mov_far[f % M_SLOTS], 16)

            def dense_in(i):
                sp.wait_ge(s_sums_out, (i + 1) * NGROUPS)
                sp.sem_inc(s_dense_open, 1)
                for b in range(4):
                    sp.dma_start(sums_sb[32 * b + SPARE_AT:32 * (b + 1), NGROUPS - 1, :],
                                 dense_t[b * SPARE:(b + 1) * SPARE, bass.ds(i * CHUNK, CHUNK)]).then_inc(s_dense, 16)

            def turn(now, steps):
                for kind, back, n in steps:
                    i = now - back
                    first, last = (isinstance(now, int) and now == end for end in (0, NCHUNKS))
                    if kind == "piece_lo":
                        if n + RAW_SLOTS < PIECES:
                            load_raw(n + RAW_SLOTS)
                        store_split(n)
                    elif kind == "split":
                        spread_far(i, n)
                    elif kind == "block" and any(place % PIECE_BLOCKS == 1 for place in places_of(n)):
                        p = places_of(n)[-1] // PIECE_BLOCKS + K_LOADS - 1
                        if p < PIECES and not first:
                            load_split(i, p)
                        elif p > PIECES and not last:
                            if p == PIECES + 1:
                                load_split(now, 0)
                            load_split(now, p - PIECES)
                    elif kind == "sum" and back and n == NQUADS - 1:
                        dense_in(i)

            for p in range(RAW_SLOTS):
                load_raw(p)
            run_turns(sp, turn)
            sp.wait_ge(s_layer_out, NCHUNKS * NOUTS)
            sp.dma_start(out, y_sb[:]).then_inc(s_stored, 16)
            sp.wait_ge(s_stored, 16)

        @block.gpsimd
        def _(pool):
            pool.wait_ge(s_consts, 1)
            nc.gpsimd.affine_select(out=ident[:], in_=ident[:], compare_op=ALU.not_equal, fill=1.0,
                                    base=0, pattern=[[-1, P]], channel_multiplier=1).then_inc(s_ident, 1)
            pool.wait_ge(s_ids, 16)

            def split_piece(p):
                slot = p % K_SLOTS
                pool.wait_ge(s_k_hi, p + 1)
                nc.gpsimd.tensor_tensor(k_ring[EMB:P, slot, :], k_raw[:, p % RAW_SLOTS, :],
                                        k_ring[0:EMB, slot, :].bitcast(fp32), ALU.subtract).then_inc(s_k_lo_gps, 1)

            def gather_chunk(i):
                for f in range(NUM_FIELDS):
                    wait(pool, s_gathered[f], i * (16 * TILES))
                nc.gpsimd.tensor_copy(ids_now[:], ids_sb[:, bass.ds(i * TILES, TILES), :]).then_inc(s_ids_now, 1)
                pool.wait_ge(s_ids_now, i + 1)
                for f in range(NUM_FIELDS):
                    if f % 2 == 0:
                        wait(pool, s_transposed, (i - 1) * NDOUBLES + f // 2 + 1)
                        pool.sem_inc(s_emb_open, 1)
                    for t in range(TILES):
                        nc.gpsimd.indirect_dma_start(
                            emb[:, f // 2, t, f % 2, :], None, tables[f],
                            bass.IndirectOffsetOnAxis(ap=ids_now[:, t, f:f + 1].bitcast(u32), axis=0),
                        ).then_inc(s_gathered[f], 16)
                    if isinstance(i, int):
                        for p in gpsimd_piece_after(f):
                            split_piece(p)

            gather_chunk(0)
            pool.wait_ge(s_k_lo_gps, len(GPSIMD_PIECES))
            with pool.Fori(1, NCHUNKS) as i:
                gather_chunk(i)

        @block.scalar
        def _(act):
            factors = (
                (w_cols_sb, w_cols.rearrange("(k p) n -> p k n", p=P)),
                (w1_sb, w_top1[0:D1, :].rearrange("(k p) n -> p k n", p=P)),
                (l0_b_sb[:], l0_b),
                (b1_sb[:], b_top1),
            )
            for dst, src in factors:
                act.dma_start(dst, src).then_inc(s_factors, 16)
            weights = [
                (w2_sb[:], w_top2.rearrange("(g p) n -> p g n", p=P)),
                (w3_sb[:], w_top3),
                (b2_sb[:], b_top2),
            ]
            for b in range(4):
                weights.append((w_comb_sb[32 * b + SPARE_AT:32 * (b + 1), NGROUPS - 1, :],
                                w_top1[D1 + b * SPARE:D1 + (b + 1) * SPARE, :]))
            for dst, src in weights:
                act.dma_start(dst, src).then_inc(s_weights, 16)

            def split_piece(p):
                slot = p % K_SLOTS
                act.wait_ge(s_raw[p % RAW_SLOTS], 16 * (p // RAW_SLOTS + 1))
                wait(act, s_bilinear, piece_done(p - K_SLOTS))
                wait(act, s_k_stored[slot], 16 * (p // K_SLOTS))
                nc.scalar.activation(k_ring[0:EMB, slot, :], k_raw[:, p % RAW_SLOTS, :],
                                     ACT.Copy).then_inc(s_k_hi, 1)

            def transposed_out(i, j):
                bank = j % TP_BANKS
                act.wait_ge(s_transposed, i * NDOUBLES + j + 1)
                old = 2 * (j - TP_BANKS) + 1
                wait(act, s_mov, i * NMOV + old)
                for f in (old - 1, old):
                    if f > 0:
                        act.wait_ge(s_mov_far[f % M_SLOTS], mov_far_count(i, f))
                    else:
                        wait(act, s_mov_far[(f + NUM_FIELDS) % M_SLOTS], mov_far_count(i - 1, f % NUM_FIELDS)
                             if f % NUM_FIELDS else 0)
                nc.scalar.activation(parts[:, bank, 0, :], transposed[:, bank, :], ACT.Copy).then_inc(s_hi, 1)
                wait(act, s_prod, (i - 1) * NBLOCKS + FIRST_BLOCK[NUM_FIELDS - 1] + min(j, NDOUBLES - 2) + 1)
                nc.scalar.activation(emb_t[:, j, :], transposed[:, bank, :], ACT.Copy).then_inc(s_emb_t, 1)

            def spread(i, j):
                bank = j % TP_BANKS
                act.wait_ge(s_hi, i * NDOUBLES + j + 1)
                act.wait_ge(s_lo, i * NDOUBLES + j + 1)
                for f in (2 * j, 2 * j + 1):
                    if f == 0:
                        continue
                    wait(act, *mov_open(i, f))
                    near, _ = halves(f)
                    nc.scalar.activation(mov[near, f % M_SLOTS, :, :], parts[near, bank, :, :].bitcast(fp32),
                                         ACT.Copy).then_inc(s_mov, 1)

            def group_out(i, g):
                act.wait_ge(s_summed, i * NQUADS + min(GROUP_QUADS * (g + 1), NQUADS))
                if g == 0:
                    wait(act, s_layer, (i - 1) * NOUTS + H1_OUTS)
                nc.scalar.activation(sums_sb[:, g, :], sums[:, g % SUM_BANKS, :], ACT.Copy).then_inc(s_sums_out, 1)

            def layer_out(i, k):
                act.wait_ge(s_layer, i * NOUTS + k + 1)
                source = layer_target(i, k)
                if k < H1_OUTS:
                    nc.scalar.activation(h1_sb[:, k, :], source, ACT.Relu,
                                         bias=b_comb_sb[:, k:k + 1]).then_inc(s_layer_out, 1)
                elif k < H2_OUTS:
                    m = k - H1_OUTS
                    nc.scalar.activation(h2_sb[:, m, :], source, ACT.Relu,
                                         bias=b2_sb[:, m:m + 1]).then_inc(s_layer_out, 1)
                else:
                    nc.scalar.activation(y_sb[:, bass.ds(i * CHUNK, CHUNK)], source[0:1, :],
                                         ACT.Copy).then_inc(s_layer_out, 1)

            def turn(now, steps):
                for kind, back, n in steps:
                    i = now - back
                    if kind == "piece_hi":
                        split_piece(n)
                    elif kind == "transpose":
                        transposed_out(i, n)
                    elif kind == "split":
                        spread(i, n)
                    elif kind == "sum" and ((n + 1) % GROUP_QUADS == 0 or n == NQUADS - 1):
                        group_out(i, n // GROUP_QUADS)
                    elif kind == "layer" and n[1] == LAYER_TERMS[n[0]] - 1:
                        layer_out(i, n[0])

            run_turns(act, turn)

        @block.vector
        def _(dve):
            nc.vector.memset(ident[:], 0.0).then_inc(s_consts, 1)
            nc.vector.memset(pair_sel[:], 0.0).then_inc(s_consts, 1)
            dve.wait_ge(s_consts, 2)
            nc.vector.memset(pair_sel[0:EMB, 30:31], 1.0).then_inc(s_consts, 1)
            nc.vector.memset(pair_sel[EMB:P, 31:32], 1.0).then_inc(s_consts, 1)

            def split_piece(p):
                slot = p % K_SLOTS
                dve.wait_ge(s_k_hi, p + 1)
                nc.vector.tensor_tensor(k_ring[EMB:P, slot, :], k_raw[:, p % RAW_SLOTS, :],
                                        k_ring[0:EMB, slot, :].bitcast(fp32), ALU.subtract).then_inc(s_k_lo, 1)

            for p in range(SPLIT_AHEAD):
                split_piece(p)

            dve.wait_ge(s_factors, 16 * 4)
            dve.wait_ge(s_folded, 1)
            nc.vector.tensor_tensor(b_comb_sb[:], transposed[:, 0, 0:H1 // P], b1_sb[:],
                                    ALU.add).then_inc(s_folded_out, 1)
            for at, g in enumerate(reversed(range(NGROUPS))):
                dve.wait_ge(s_folded, at + 2)
                if g == NGROUPS - 1:
                    parts_out = [slice(32 * b, 32 * b + SPARE_AT) for b in range(4)]
                else:
                    parts_out = [slice(0, P)]
                for rows in parts_out:
                    last = nc.vector.tensor_copy(w_comb_sb[rows, g, :], bilinear[rows, g, :])
                last.then_inc(s_folded_out, 1)

            def split_double(i, j):
                bank = j % TP_BANKS
                dve.wait_ge(s_hi, i * NDOUBLES + j + 1)
                dve.wait_ge(s_emb_t, i * NDOUBLES + j + 1)
                nc.vector.tensor_tensor(parts[:, bank, 1, :], emb_t[:, j, :],
                                        parts[:, bank, 0, :].bitcast(fp32), ALU.subtract).then_inc(s_lo, 1)

            def multiply(i, n):
                c, j = BLOCKS[n]
                if n == FIRST_BLOCK[c]:
                    dve.wait_ge(s_emb_t, i * NDOUBLES + c // 2 + 1)
                if n % 4 == 0:
                    wait(dve, s_summed, i * NQUADS + n // 4 - X_SLOTS + 1)
                dve.wait_ge(s_bilinear, i * NBLOCKS + n + 1)
                halves = [(slice(0, P), j)]
                if j is None:
                    halves = [(slice(0, EMB), c // 2 - 1), (slice(EMB, P), c // 2)]
                for rows, double in halves:
                    last = nc.vector.tensor_tensor(prod[rows, prod_slot(n), n % 4, :], bilinear[rows, n % T_BANKS, :],
                                                   emb_t[rows, double, :], ALU.mult)
                last.then_inc(s_prod, 1)

            def turn(now, steps):
                for kind, back, n in steps:
                    i = now - back
                    if kind == "piece_lo" and n >= SPLIT_AHEAD and n not in GPSIMD_PIECES:
                        split_piece(n)
                    elif kind == "split":
                        split_double(i, n)
                    elif kind == "block":
                        multiply(i, n)

            run_turns(dve, turn)

        @block.tensor
        def _(pe):
            pe.wait_ge(s_consts, 4)
            pe.wait_ge(s_ident, 1)
            pe.wait_ge(s_factors, 16 * 4)
            for m in range(H1 // P):
                for k in range(D1 // P):
                    last = nc.tensor.matmul(transposed[:, 0, m:m + 1], w1_sb[:, k, m * P:(m + 1) * P],
                                            l0_b_sb[:, k:k + 1], start=k == 0, stop=k == D1 // P - 1)
            last.then_inc(s_folded, 1)
            for g in reversed(range(NGROUPS)):
                for k in range(D1 // P):
                    last = nc.tensor.matmul(bilinear[:, g, :], w_cols_sb[:, k, g * P:(g + 1) * P], w1_sb[:, k, :],
                                            start=k == 0, stop=k == D1 // P - 1)
                last.then_inc(s_folded, 1)
            pe.wait_ge(s_folded_out, 1 + NGROUPS)
            pe.wait_ge(s_weights, 16 * 7)

            def transpose_double(i, j):
                pe.wait_ge(s_gathered[2 * j], (i + 1) * (16 * TILES))
                pe.wait_ge(s_gathered[2 * j + 1], (i + 1) * (16 * TILES))
                wait(pe, s_emb_t, i * NDOUBLES + j - TP_BANKS + 1)
                for t in range(TILES):
                    last = nc.tensor.transpose(transposed[:, j % TP_BANKS, t * P:(t + 1) * P],
                                               emb[:, j, t, :, :], ident[:])
                last.then_inc(s_transposed, 1)

            def bilinear_block(now, i, n):
                c, j = BLOCKS[n]
                places = places_of(n)
                for piece in (place // PIECE_BLOCKS for place in places if place % PIECE_BLOCKS == 0):
                    if isinstance(i, int) and i == 0:
                        pe.wait_ge(*k_split(piece))
                    else:
                        pe.wait_ge(s_k_loaded[piece % K_SLOTS],
                                   ((i - 1) * (PIECES // K_SLOTS) + piece // K_SLOTS + 1) * 16)
                if n == FIRST_BLOCK[c]:
                    pe.wait_ge(s_mov, i * NMOV + c)
                    pe.wait_ge(s_mov_far[c % M_SLOTS], mov_far_count(i, c))
                if j is None:
                    pe.wait_ge(s_mov_far[(c - 1) % M_SLOTS], mov_far_count(i, c - 1))
                wait(pe, s_prod, i * NBLOCKS + n - T_BANKS + 1)
                fields = (c,) if j is not None else (c - 1, c)
                products = [(field, place, part) for part in range(2) for field, place in zip(fields, places)]
                for field, place, part in products:
                    piece, col = place // PIECE_BLOCKS, place % PIECE_BLOCKS * P
                    last = nc.tensor.matmul(bilinear[:, n % T_BANKS, :], k_ring[:, piece % K_SLOTS, col:col + P],
                                            mov[:, field % M_SLOTS, part, :],
                                            start=(field, place, part) == products[0],
                                            stop=(field, place, part) == products[-1])
                last.then_inc(s_bilinear, 1)

            def sum_quad(i, quad):
                g, pos = divmod(quad, GROUP_QUADS)
                if pos == 0:
                    wait(pe, s_sums_out, i * NGROUPS + g - SUM_BANKS + 1)
                    outs = sum(layer_phase(k) < g for k in range(NOUTS))
                    wait(pe, s_layer_out, (i - 1) * NOUTS + outs)
                pe.wait_ge(s_prod, i * NBLOCKS + 4 * quad + 4)
                for b in range(4):
                    last = nc.tensor.matmul(sums[32 * b:32 * b + 32, g % SUM_BANKS, :],
                                            pair_sel[:, 30 - 2 * pos:62 - 2 * pos],
                                            prod[:, prod_slot(4 * quad), b, :],
                                            start=pos == 0, stop=pos == GROUP_QUADS - 1 or quad == NQUADS - 1,
                                            tile_position=(0, 32 * b))
                last.then_inc(s_summed, 1)

            def layer(i, k, term):
                last_term = term == LAYER_TERMS[k] - 1
                if term == 0 and isinstance(i, int):
                    pe.wait_ge(s_sums_out, (i + 1) * NGROUPS)
                    pe.wait_ge(s_prod, (i + 1) * NBLOCKS)
                    if k >= T_BANKS:
                        pe.wait_ge(s_layer_out, i * NOUTS + k - T_BANKS + 1)
                elif term == 0:
                    pe.wait_ge(s_sums_out, (i + 1) * NGROUPS + layer_phase(k))
                    if k:
                        pe.wait_ge(s_layer_out, i * NOUTS + k)
                if k in (H1_OUTS, H2_OUTS) and term == 0:
                    pe.wait_ge(s_layer_out, i * NOUTS + k)
                if k == 0 and term == NGROUPS - 1:
                    pe.wait_ge(s_dense, (i + 1) * (16 * 4))
                if k < H1_OUTS:
                    weights, x = w_comb_sb[:, term, k * P:(k + 1) * P], sums_sb[:, term, :]
                elif k < H2_OUTS:
                    weights, x = w2_sb[:, term, (k - H1_OUTS) * P:(k - H1_OUTS + 1) * P], h1_sb[:, term, :]
                else:
                    weights, x = w3_sb[:, term:term + 1], h2_sb[:, term, :]
                last = nc.tensor.matmul(layer_target(i, k)[0:weights.shape[1], :], weights, x,
                                        start=term == 0, stop=last_term)
                if last_term:
                    last.then_inc(s_layer, 1)

            def turn(now, steps):
                for kind, back, n in steps:
                    i = now - back
                    if kind == "transpose":
                        transpose_double(i, n)
                    elif kind == "block":
                        bilinear_block(now, i, n)
                    elif kind == "sum":
                        sum_quad(i, n)
                    elif kind == "layer":
                        layer(i, *n)

            run_turns(pe, turn)


def kernel(**inputs):
    import numpy as np
    import concourse.bacc as bacc
    from concourse.bass_utils import run_bass_kernel_spmd

    nc = bacc.Bacc("TRN2", target_bir_lowering=False, num_devices=1)
    arrays = {}

    def give(name, a):
        a = np.ascontiguousarray(a)
        arrays[name] = a
        return nc.dram_tensor(name, a.shape, mybir.dt.from_np(a.dtype), kind="ExternalInput").ap()

    def columns(v):
        return np.asarray(v).reshape(-1, P).T

    tables = [give(f"table_{f}", inputs[f"tbl_{f}"]) for f in range(NUM_FIELDS)]
    ids = give("ids", inputs["ids"])
    dense_t = give("dense_t", np.asarray(inputs["dense_ctx"]).T)
    k = np.asarray(inputs["L0_rec_kernel"])
    operands = np.zeros((EMB, len(PLACES), 2, EMB), k.dtype)
    for n in range(NBLOCKS):
        places = places_of(n)
        low, high = (k[:, pair_index(*pair), :] for pair in block_pairs(n))
        operands[:, places[0], 0] = low
        operands[:, places[-1], 1] = high.T if BLOCKS[n][1] is None else high
    kernel_blocks = give("kernel_blocks", operands.reshape(EMB, PIECES * PIECE))
    w_cols = give("w_cols", np.asarray(inputs["L0_rec_W"])[:, slot_pairs()])
    l0_b = give("l0_b", columns(inputs["L0_rec_b"]))
    w_top1 = give("w_top1", inputs["W_top1"])
    b_top1 = give("b_top1", columns(inputs["b_top1"]))
    w_top2 = give("w_top2", inputs["W_top2"])
    b_top2 = give("b_top2", columns(inputs["b_top2"]))
    w_top3 = give("w_top3", columns(inputs["W_top3"]))
    out = nc.dram_tensor("out", (1, BATCH), mybir.dt.float32, kind="ExternalOutput").ap()
    build(nc, tables, ids, dense_t, kernel_blocks, w_cols, l0_b, w_top1, b_top1, w_top2, b_top2, w_top3, out)
    r = run_bass_kernel_spmd(nc, [arrays], core_ids=[0])
    return np.asarray(r.results[0]["out"]).reshape(BATCH, 1)
```
